# Optimizing a Trainium2 kernel written in Bass

```python
import numpy as np
import jax
import jax.numpy as jnp

def _softmax(x, axis=-1):
    return jax.nn.softmax(x, axis=axis)

def _gelu(x):
    return jax.nn.gelu(x, approximate=True)

def _silu(x):
    return jax.nn.silu(x)

def _sigmoid(x):
    return jax.nn.sigmoid(x)

def _layernorm(x, axis=-1, eps=1e-05):
    m = jnp.mean(x, axis=axis, keepdims=True)
    v = jnp.var(x, axis=axis, keepdims=True)
    return (x - m) / jnp.sqrt(v + eps)

def _scatter_add(tgt, idx, src, axis=0):
    return tgt.at[idx].add(src)

def _segment_sum(src, seg, n):
    return jax.ops.segment_sum(src, seg, n)
kernel_name = 'mk_prb_d1_jaxref_r4_9bbe10'

def setup_inputs(seed: int=0):
    np.random.seed(seed)
    _w = jnp.asarray

    def _L0_attn_setup():
        import jax, jax.numpy as jnp
        import numpy as np
        D_MODEL = 512
        N_HEADS = 16
        N_KV_HEADS = 2
        D_HEAD = D_MODEL // N_HEADS
        N_GROUPS = N_HEADS // N_KV_HEADS
        B, T = (2, 512)
        key = jax.random.key(seed)
        ks = jax.random.split(key, 9)
        s = 0.02
        return {'x': jax.random.normal(ks[0], (B, T, D_MODEL), jnp.float32), 'Wq': jax.random.normal(ks[1], (D_MODEL, N_HEADS * D_HEAD), jnp.float32) * s, 'bq': jnp.zeros((N_HEADS * D_HEAD,), jnp.float32), 'Wk': jax.random.normal(ks[2], (D_MODEL, N_KV_HEADS * D_HEAD), jnp.float32) * s, 'bk': jnp.zeros((N_KV_HEADS * D_HEAD,), jnp.float32), 'Wv': jax.random.normal(ks[3], (D_MODEL, N_KV_HEADS * D_HEAD), jnp.float32) * s, 'bv': jnp.zeros((N_KV_HEADS * D_HEAD,), jnp.float32), 'Wo': jax.random.normal(ks[4], (D_MODEL, D_MODEL), jnp.float32) * s, 'bo': jnp.zeros((D_MODEL,), jnp.float32)}
    _L0_attn_in = _L0_attn_setup()

    def _L0_ffn_setup():
        import jax, jax.numpy as jnp
        import numpy as np
        B, S, D = (4, 128, 512)
        E, K, H = (8, 2, 352)
        HS = 2 * 352
        ALPHA = 0.001
        W_SCALE = 0.02

        def _moe_forward(hidden_states, gate_w, w_gate, w_up, w_down, sw_gate, sw_up, sw_down):
            b, s, d = hidden_states.shape
            x = hidden_states.reshape(-1, d)
            T = x.shape[0]
            logits = x @ gate_w
            scores = jax.nn.softmax(logits, axis=-1)
            topk_w, topk_idx = jax.lax.top_k(scores, K)
            mask = jax.nn.one_hot(topk_idx, E, dtype=scores.dtype).sum(axis=1)
            ce = mask.mean(axis=0)
            Pi = scores.mean(axis=0)
            aux_loss = (Pi * ce * E).sum() * ALPHA
            comb = jnp.zeros((T, E), dtype=x.dtype)
            comb = comb.at[jnp.arange(T)[:, None], topk_idx].add(topk_w)
            g = jax.nn.silu(jnp.einsum('td,edh->teh', x, w_gate)) * jnp.einsum('td,edh->teh', x, w_up)
            routed = jnp.einsum('teh,ehd,te->td', g, w_down, comb)
            shared = jax.nn.silu(x @ sw_gate) * (x @ sw_up) @ sw_down
            out = (routed + shared).reshape(b, s, d)
            return (out, aux_loss)
        key = jax.random.key(seed)
        ks = jax.random.split(key, 8)
        rn = lambda k, sh: jax.random.normal(k, sh, dtype=jnp.float32)
        return {'hidden_states': rn(ks[0], (B, S, D)), 'gate_w': rn(ks[1], (D, E)) * W_SCALE, 'w_gate': rn(ks[2], (E, D, H)) * W_SCALE, 'w_up': rn(ks[3], (E, D, H)) * W_SCALE, 'w_down': rn(ks[4], (E, H, D)) * W_SCALE, 'sw_gate': rn(ks[5], (D, HS)) * W_SCALE, 'sw_up': rn(ks[6], (D, HS)) * W_SCALE, 'sw_down': rn(ks[7], (HS, D)) * W_SCALE}
    _L0_ffn_in = _L0_ffn_setup()
    _d = {'L0_attn_x': _L0_attn_in['x'], 'L0_attn_Wq': _L0_attn_in['Wq'], 'L0_attn_bq': _L0_attn_in['bq'], 'L0_attn_Wk': _L0_attn_in['Wk'], 'L0_attn_bk': _L0_attn_in['bk'], 'L0_attn_Wv': _L0_attn_in['Wv'], 'L0_attn_bv': _L0_attn_in['bv'], 'L0_attn_Wo': _L0_attn_in['Wo'], 'L0_attn_bo': _L0_attn_in['bo'], 'L0_ffn_gate_w': _L0_ffn_in['gate_w'], 'L0_ffn_w_gate': _L0_ffn_in['w_gate'], 'L0_ffn_w_up': _L0_ffn_in['w_up'], 'L0_ffn_w_down': _L0_ffn_in['w_down'], 'L0_ffn_sw_gate': _L0_ffn_in['sw_gate'], 'L0_ffn_sw_up': _L0_ffn_in['sw_up'], 'L0_ffn_sw_down': _L0_ffn_in['sw_down']}
    _x0 = _d['L0_attn_x']
    _d['L0_attn_x'] = jax.random.normal(jax.random.fold_in(jax.random.key(seed), 1), (2, 2048, 512), dtype=_x0.dtype)
    del _x0
    return _d

def reference(L0_attn_x, L0_attn_Wq, L0_attn_bq, L0_attn_Wk, L0_attn_bk, L0_attn_Wv, L0_attn_bv, L0_attn_Wo, L0_attn_bo, L0_ffn_gate_w, L0_ffn_w_gate, L0_ffn_w_up, L0_ffn_w_down, L0_ffn_sw_gate, L0_ffn_sw_up, L0_ffn_sw_down):

    def _L0_attn_ref(x, Wq, bq, Wk, bk, Wv, bv, Wo, bo):
        import jax, jax.numpy as jnp
        import numpy as np
        D_MODEL = 512
        N_HEADS = 16
        N_KV_HEADS = 2
        D_HEAD = D_MODEL // N_HEADS
        N_GROUPS = N_HEADS // N_KV_HEADS
        B, T = (2, 512)
        Bx, Tx, C = x.shape
        Q = (x @ Wq + bq).reshape(Bx, Tx, N_HEADS, D_HEAD)
        K = (x @ Wk + bk).reshape(Bx, Tx, N_KV_HEADS, D_HEAD)
        V = (x @ Wv + bv).reshape(Bx, Tx, N_KV_HEADS, D_HEAD)
        Qg = Q.reshape(Bx, Tx, N_KV_HEADS, N_GROUPS, D_HEAD)
        scale = jnp.sqrt(jnp.float32(D_HEAD))
        scores = jnp.einsum('bqkgd,bskd->bkgqs', Qg, K) / scale
        causal = jnp.triu(jnp.ones((Tx, Tx), bool), k=1)
        scores = jnp.where(causal, -jnp.inf, scores)
        attn = jax.nn.softmax(scores, axis=-1)
        out = jnp.einsum('bkgqs,bskd->bqkgd', attn, V).reshape(Bx, Tx, C)
        return out @ Wo + bo

    def _L0_ffn_ref(hidden_states, gate_w, w_gate, w_up, w_down, sw_gate, sw_up, sw_down):
        import jax, jax.numpy as jnp
        import numpy as np
        B, S, D = (4, 128, 512)
        E, K, H = (8, 2, 352)
        HS = 2 * 352
        ALPHA = 0.001
        W_SCALE = 0.02

        def _moe_forward(hidden_states, gate_w, w_gate, w_up, w_down, sw_gate, sw_up, sw_down):
            b, s, d = hidden_states.shape
            x = hidden_states.reshape(-1, d)
            T = x.shape[0]
            logits = x @ gate_w
            scores = jax.nn.softmax(logits, axis=-1)
            topk_w, topk_idx = jax.lax.top_k(scores, K)
            mask = jax.nn.one_hot(topk_idx, E, dtype=scores.dtype).sum(axis=1)
            ce = mask.mean(axis=0)
            Pi = scores.mean(axis=0)
            aux_loss = (Pi * ce * E).sum() * ALPHA
            comb = jnp.zeros((T, E), dtype=x.dtype)
            comb = comb.at[jnp.arange(T)[:, None], topk_idx].add(topk_w)
            g = jax.nn.silu(jnp.einsum('td,edh->teh', x, w_gate)) * jnp.einsum('td,edh->teh', x, w_up)
            routed = jnp.einsum('teh,ehd,te->td', g, w_down, comb)
            shared = jax.nn.silu(x @ sw_gate) * (x @ sw_up) @ sw_down
            out = (routed + shared).reshape(b, s, d)
            return (out, aux_loss)
        out, _aux = _moe_forward(hidden_states, gate_w, w_gate, w_up, w_down, sw_gate, sw_up, sw_down)
        return out
    x = L0_attn_x
    xn = _layernorm(x, axis=-1)
    x = x + _L0_attn_ref(xn, L0_attn_Wq, L0_attn_bq, L0_attn_Wk, L0_attn_bk, L0_attn_Wv, L0_attn_bv, L0_attn_Wo, L0_attn_bo) + _L0_ffn_ref(xn, L0_ffn_gate_w, L0_ffn_w_gate, L0_ffn_w_up, L0_ffn_w_down, L0_ffn_sw_gate, L0_ffn_sw_up, L0_ffn_sw_down)
    return x

_drawn_inputs = setup_inputs


def setup_inputs(seed=0):
    import zlib

    import numpy as np

    out = dict(_drawn_inputs(seed))
    spreads = {'L0_attn_bq': (0.0, 0.8),
     'L0_attn_bk': (0.0, 2.0),
     'L0_attn_bv': (0.0, 0.776),
     'L0_attn_bo': (0.0, 0.37)}
    factors = {'L0_attn_Wq': 8.0,
     'L0_attn_Wk': 8.0,
     'L0_attn_Wv': 4.144,
     'L0_ffn_gate_w': 5.598,
     'L0_ffn_w_gate': 4.959,
     'L0_ffn_w_up': 4.859,
     'L0_ffn_w_down': 4.849,
     'L0_ffn_sw_gate': 4.476,
     'L0_ffn_sw_up': 4.376,
     'L0_ffn_sw_down': 4.381}
    for name, (base, spread) in spreads.items():
        noise = np.random.default_rng([zlib.crc32(name.encode()), seed]).standard_normal(out[name].shape)
        drawn = base * np.exp(spread * noise) if base else spread * noise
        out[name] = jnp.asarray(drawn.astype(out[name].dtype))
    for name, factor in factors.items():
        out[name] = (out[name] * factor).astype(out[name].dtype)
    return out
```

```python
from contextlib import ExitStack

import concourse.bass as bass
from concourse import mybir
from concourse.alu_op_type import AluOpType as ALU

ACT = mybir.ActivationFunctionType
AX = mybir.AxisListType
F32 = mybir.dt.float32
F32R = mybir.dt.float32r
BF16 = mybir.dt.bfloat16
I32 = mybir.dt.int32

P = 128
MASKED = -3.0e38
EPS = 1e-5


def layer_kernel(nc, x, Wq, bq, Wk, bk, Wv, bv, Wo, bo, gate_w, w_gate, w_up, w_down,
                 sw_gate, sw_up, sw_down, out):
    B, T, D = x.shape
    E, _, H = w_gate.shape
    HS = sw_gate.shape[1]
    KV = Wk.shape[1]
    DH = 32
    NKV = KV // DH
    TILES = B * T // P
    DK = D // P
    HC = -(-H // P)
    SC = -(-HS // P)
    H_REST = H - (HC - 1) * P
    S_REST = HS - (SC - 1) * P
    SLOT_TILES = 2 * B * T // P + E
    HG = P // DH
    GROUPS = D // P
    QB = 512
    NQB = T // QB
    KT = T // P
    SCALE = float(DH) ** -0.5
    KROWS = 3 * DH
    QROWS = KROWS + 2
    C_KV, C_GATE, C_END = D, D + 2 * KV, D + 2 * KV + E
    assert HG == 4 and QB == 4 * P and NKV == 2 and GROUPS == 2 * NKV and S_REST == 64

    xt = x.rearrange("b (t p) d -> (b t) p d", p=P)
    ot = out.rearrange("b (t p) d -> (b t) p d", p=P)

    def dram(name, shape, dt=F32):
        return nc.dram_tensor(name, shape, dt, kind="Internal").ap()

    xn_d = dram("xn_scratch", (TILES * P, D))
    q_d = dram("q_scratch", (TILES, P, D))
    k_d = dram("k_scratch", (KROWS, B * NKV, T))
    y_d = dram("y_scratch", (TILES, P, D))
    slot_d = dram("slot_token_scratch", (SLOT_TILES * P, 1), I32)
    ys_d = dram("slot_out_scratch", (SLOT_TILES * P, D))
    at_d = dram("attention_scratch", (B * GROUPS, P, T))
    xn_t = xn_d.rearrange("(t p) d -> t p d", p=P)
    ys_t = ys_d.rearrange("(t p) d -> t p d", p=P)

    def tile(view, t):
        if isinstance(t, int):
            return view[t]
        return view[bass.ds(t, 1)].rearrange("a p d -> (a p) d")

    def wait(eng, sem, value):
        if not isinstance(value, int) or value > 0:
            eng.wait_ge(sem, value)

    def wait_apart(eng, sem, value, passed):
        if not isinstance(value, int) or value > 0:
            eng.wait_ge(sem, value)
            eng.sem_inc(passed, 1)

    outer = ExitStack()
    with outer:
        def keep(name, shape, dt=F32):
            return outer.enter_context(nc.sbuf_tensor(name, shape, dt))

        ident = keep("ident", [P, P])
        ident16 = keep("ident16", [P, P], BF16)
        below16 = keep("masked_above_diagonal", [P, P], BF16)
        above16 = keep("masked_below_diagonal", [P, P], BF16)
        logits = keep("logits", [P, TILES, E])
        v_all = keep("v_all", [P, TILES, KV])
        slot_of = keep("slot_of", [P, 2, TILES], I32)
        token = keep("token", [P, TILES], I32)
        row_i = keep("row_i", [P, 2, 2, TILES], I32)
        weight_of = keep("weight_of", [P, 2, TILES])
        expert_of = keep("expert_of", [P, SLOT_TILES], I32)
        slot_token = keep("slot_token", [P, SLOT_TILES], I32)

        with ExitStack() as ctx:
            def sb(name, shape, dt=F32):
                return ctx.enter_context(nc.sbuf_tensor(name, shape, dt))

            def pb(name, shape, dt=F32):
                return ctx.enter_context(nc.psum_tensor(name, shape, dt))

            def sem(name):
                return ctx.enter_context(nc.semaphore(name))

            raw_in = sb("raw_in", [P, DK, C_END])
            raw_gu = sb("raw_gu", [P, DK, 2 * HS])
            raw_dn = sb("raw_dn", [P, SC, D])
            in_h, in_l = sb("in_h", [P, DK, C_END], F32R), sb("in_l", [P, DK, C_END], F32R)
            gu_h, gu_l = sb("gu_h", [P, DK, 2 * HS], F32R), sb("gu_l", [P, DK, 2 * HS], F32R)
            dn_h, dn_l = sb("dn_h", [P, SC, D], F32R), sb("dn_l", [P, SC, D], F32R)
            bias = sb("bias", [P, C_GATE])
            bias_o = sb("bias_o", [P, D])
            xs = sb("xs", [P, D])
            xr = sb("xr", [P, D])
            stats = sb("stats", [P, 6])
            mean_var = sb("mean_var", [P, 2])
            ve = sb("ve", [P, 1])
            seed = sb("seed", [P, 1], I32)
            newton = sb("newton", [P, 3, 3])
            xn = sb("xn", [P, D])
            xT_h, xT_l = sb("xT_h", [P, DK, P], F32R), sb("xT_l", [P, DK, P], F32R)
            q_sb = sb("q_sb", [P, D])
            k_raw = sb("k_raw", [P, NKV, DH])
            k_aug = sb("k_aug", [P, NKV, KROWS], F32R)
            k_sb = sb("k_sb", [KROWS, NKV, P], F32R)
            act_g = sb("act_g", [P, HS])
            h = sb("h", [P, SC * P])
            hT_h, hT_l = sb("hT_h", [P, SC, P], F32R), sb("hT_l", [P, SC, P], F32R)
            y_sb = sb("y_sb", [P, D])

            p_x = pb("p_x", [P, DK, P])
            p_q = pb("p_q", [P, D])
            p_kv = pb("p_kv", [P, 512])
            p_gu = pb("p_gu", [P, 4, 512])
            p_dn = pb("p_dn", [P, D])
            p_g, p_u = p_gu[:, 0:2, 0:HS // 2], p_gu[:, 2:4, 0:HS // 2]
            p_hT = p_gu[:, 2:4, :].rearrange("p a (b q) -> p (a b) q", q=P)
            p_kT = p_kv[0:KROWS, 256:512].rearrange("r (g t) -> r g t", g=NKV)

            w_loaded = [sem(f"w_loaded{n}") for n in range(3)]
            bias_loaded = sem("bias_loaded")
            consts = sem("consts")
            w_hi, w_lo = sem("w_hi"), sem("w_lo")
            x_loaded, xr_loaded, xr_ready = sem("x_loaded"), sem("xr_loaded"), sem("xr_ready")
            ln_step, xn_done = sem("ln_step"), sem("xn_done")
            xT_done, xTh_done, xTl_done = sem("xT_done"), sem("xTh_done"), sem("xTl_done")
            qkv_done, qkv_out, k_split = sem("qkv_done"), sem("qkv_out"), sem("k_split")
            kT_done, kT_out = sem("kT_done"), sem("kT_out")
            gu_done, silu_done, h_done = sem("gu_done"), sem("silu_done"), sem("h_done")
            hT_done, hTh_done, hTl_done = sem("hT_done"), sem("hTh_done"), sem("hTl_done")
            dn_done, y_done = sem("dn_done"), sem("y_done")
            passed = sem("passed")
            xn_stored, q_stored, k_stored, y_stored = (sem("xn_stored"), sem("q_stored"), sem("k_stored"),
                                                       sem("y_stored"))

            LN_STEPS = 14

            def steps(eng, body):
                body(0)
                with eng.Fori(1, TILES - 2) as t:
                    body(t)
                body(TILES - 2)
                body(TILES - 1)
                body(TILES)

            def has(t):
                if not isinstance(t, int):
                    return True, True, True
                return t >= 1, t < TILES, t + 1 < TILES

            block = ctx.enter_context(nc.Block())

            @block.sync
            def _(sp):
                sp.dma_start(xs[:], xt[0]).then_inc(x_loaded, 16)
                for w, c in ((Wq, 0), (Wk, D), (Wv, D + KV), (gate_w, C_GATE)):
                    sp.dma_start(raw_in[:, :, c:c + w.shape[1]],
                                 w.rearrange("(k p) n -> p k n", p=P)).then_inc(w_loaded[0], 16)
                for w, c in ((sw_gate, 0), (sw_up, HS)):
                    sp.dma_start(raw_gu[:, :, c:c + HS],
                                 w.rearrange("(k p) n -> p k n", p=P)).then_inc(w_loaded[1], 16)
                sp.dma_start(raw_dn[:, 0:SC - 1, :], sw_down[0:(SC - 1) * P, :].rearrange("(k p) n -> p k n", p=P)
                             ).then_inc(w_loaded[2], 16)
                sp.dma_start(raw_dn[0:S_REST, SC - 1, :], sw_down[(SC - 1) * P:HS, :]).then_inc(w_loaded[2], 16)

                def next_x(t):
                    sp.wait_ge(xn_done, t)
                    if not isinstance(t, int) or t < TILES:
                        sp.dma_start(xs[:], tile(xt, t)).then_inc(x_loaded, 16)
                    sp.dma_start(tile(xn_t, t - 1), xn[:]).then_inc(xn_stored, 16)

                next_x(1)

                def body(t):
                    before, here, after = has(t)
                    if after:
                        next_x(t + 2)
                    if here:
                        sp.wait_ge(qkv_out, t + 1)
                        sp.dma_start(tile(q_d, t), q_sb[:]).then_inc(q_stored, 16)
                        sp.wait_ge(kT_out, t + 1)
                        sp.dma_start(k_d[:, bass.ds(t // KT * NKV, NKV), bass.ds(t % KT * P, P)],
                                     k_sb[:].bitcast(F32)).then_inc(k_stored, 16)
                    if before:
                        sp.wait_ge(y_done, t)
                        sp.dma_start(tile(y_d, t - 1), y_sb[:]).then_inc(y_stored, 16)
                    if here:
                        sp.dma_start(xr[:], tile(xt, t)).then_inc(xr_loaded, 16)

                steps(sp, body)
                sp.wait_ge(xn_stored, 16 * TILES)
                sp.wait_ge(q_stored, 16 * TILES)
                sp.wait_ge(k_stored, 16 * TILES)
                sp.wait_ge(y_stored, 16 * TILES)

            @block.gpsimd
            def _(pool):
                for b_, c in ((bq, 0), (bk, D), (bv, D + KV)):
                    pool.dma_start(bias[:, c:c + b_.shape[0]], b_.partition_broadcast(P)).then_inc(bias_loaded, 16)
                pool.dma_start(bias_o[:], bo.partition_broadcast(P)).then_inc(bias_loaded, 16)
                pool.memset(ident[:], 0.0).then_inc(consts, 1)
                pool.memset(ident16[:], 0.0).then_inc(consts, 1)
                pool.memset(below16[:], 0.0).then_inc(consts, 1)
                pool.memset(above16[:], 0.0).then_inc(consts, 1)
                pool.memset(h[:, HS:SC * P], 0.0).then_inc(consts, 1)
                pool.wait_ge(consts, 5)
                for m in (ident, ident16):
                    pool.affine_select(out=m[:], in_=m[:], pattern=[[-1, P]], compare_op=ALU.not_equal, fill=1.0,
                                       base=0, channel_multiplier=1).then_inc(consts, 1)
                pool.affine_select(out=below16[:], in_=below16[:], pattern=[[-1, P]], compare_op=ALU.is_ge,
                                   fill=MASKED, base=0, channel_multiplier=1).then_inc(consts, 1)
                pool.affine_select(out=above16[:], in_=above16[:], pattern=[[1, P]], compare_op=ALU.is_ge,
                                   fill=MASKED, base=0, channel_multiplier=-1).then_inc(consts, 1)
                pool.wait_ge(bias_loaded, 64)

                def body(t):
                    pool.wait_ge(xr_loaded, 16 * (t + 1))
                    pool.tensor_tensor(xr[:], xr[:], bias_o[:], ALU.add).then_inc(xr_ready, 1)

                with pool.Fori(0, TILES) as t:
                    body(t)

            @block.scalar
            def _(act):
                act.wait_ge(w_loaded[0], 64)
                act.activation(in_h[:], raw_in[:], ACT.Copy).then_inc(w_hi, 1)

                def xT_hi(t):
                    act.wait_ge(xT_done, t + 1)
                    wait(act, qkv_done, t)
                    wait(act, gu_done, t)
                    act.activation(xT_h[:], p_x[:], ACT.Copy).then_inc(xTh_done, 1)

                xT_hi(0)
                act.wait_ge(w_loaded[1], 32)
                act.activation(gu_h[:], raw_gu[:], ACT.Copy).then_inc(w_hi, 1)
                act.wait_ge(w_loaded[2], 32)
                act.activation(dn_h[:, 0:SC - 1, :], raw_dn[:, 0:SC - 1, :], ACT.Copy).then_inc(w_hi, 1)
                act.activation(dn_h[0:S_REST, SC - 1, :], raw_dn[0:S_REST, SC - 1, :], ACT.Copy).then_inc(w_hi, 1)

                def body(t):
                    before, here, after = has(t)
                    if before:
                        act.wait_ge(hT_done, t)
                        act.activation(hT_h[:], p_hT[:, 0:SC, :], ACT.Copy).then_inc(hTh_done, 1)
                    if here:
                        act.wait_ge(gu_done, t + 1)
                        wait(act, h_done, t)
                        act.activation(act_g[:].rearrange("p (a n) -> p a n", a=2), p_g,
                                       ACT.Silu).then_inc(silu_done, 1)
                        act.wait_ge(kT_done, t + 1)
                        wait(act, k_stored, 16 * t)
                        act.activation(k_sb[:], p_kT, ACT.Copy).then_inc(kT_out, 1)
                    if after:
                        xT_hi(t + 1)

                steps(act, body)

            @block.vector
            def _(dve):
                def normalise(t):
                    base = LN_STEPS * t
                    n = 0

                    def done(ins):
                        nonlocal n
                        n += 1
                        ins.then_inc(ln_step, 1)
                        dve.wait_ge(ln_step, base + n)

                    dve.wait_ge(x_loaded, 16 * (t + 1))
                    done(dve.bn_stats(stats[:], xs[:]))
                    dve.sem_inc(passed, 1)
                    done(dve.bn_aggr(mean_var[:], stats[:]))
                    done(dve.tensor_scalar_add(ve[:], mean_var[:, 1:2], EPS))
                    done(dve.tensor_scalar(seed[:], ve[:].bitcast(I32), 1, None, ALU.logical_shift_right))
                    done(dve.tensor_scalar(seed[:], seed[:], -1.0, float(0x5F3759DF), ALU.mult, ALU.add))
                    y = seed[:].bitcast(F32)
                    for i in range(3):
                        done(dve.scalar_tensor_tensor(out=newton[:, i, 0:1], in0=y, scalar=y, in1=ve[:],
                                                      op0=ALU.mult, op1=ALU.mult))
                        done(dve.tensor_scalar(newton[:, i, 1:2], newton[:, i, 0:1], -0.5, 1.5, ALU.mult, ALU.add))
                        done(dve.tensor_tensor(newton[:, i, 2:3], newton[:, i, 1:2], y, ALU.mult))
                        y = newton[:, i, 2:3]
                    assert n == LN_STEPS
                    wait(dve, xT_done, t)
                    wait(dve, xn_stored, 16 * t)
                    dve.tensor_scalar(xn[:], xs[:], mean_var[:, 0:1], y, ALU.subtract, ALU.mult).then_inc(xn_done, 1)

                def xT_lo(t):
                    dve.wait_ge(xTh_done, t + 1)
                    dve.tensor_tensor(xT_l[:], p_x[:], xT_h[:], ALU.subtract).then_inc(xTl_done, 1)

                normalise(0)
                dve.wait_ge(w_hi, 1)
                dve.tensor_tensor(in_l[:], raw_in[:], in_h[:], ALU.subtract).then_inc(w_lo, 1)
                xT_lo(0)
                dve.wait_ge(w_hi, 2)
                dve.tensor_tensor(gu_l[:], raw_gu[:], gu_h[:], ALU.subtract).then_inc(w_lo, 1)
                dve.wait_ge(w_hi, 4)
                dve.tensor_tensor(dn_l[:, 0:SC - 1, :], raw_dn[:, 0:SC - 1, :], dn_h[:, 0:SC - 1, :],
                                  ALU.subtract).then_inc(w_lo, 1)
                dve.tensor_tensor(dn_l[0:S_REST, SC - 1, :], raw_dn[0:S_REST, SC - 1, :],
                                  dn_h[0:S_REST, SC - 1, :], ALU.subtract).then_inc(w_lo, 1)
                dve.wait_ge(bias_loaded, 64)
                dve.wait_ge(consts, 9)

                def body(t):
                    before, here, after = has(t)
                    if before:
                        dve.wait_ge(hTh_done, t)
                        dve.tensor_tensor(hT_l[:], p_hT[:, 0:SC, :], hT_h[:], ALU.subtract).then_inc(hTl_done, 1)
                    if here:
                        dve.wait_ge(qkv_done, t + 1)
                        wait(dve, kT_done, t)
                        dve.tensor_tensor(k_raw[:], p_kv[:, 0:KV].rearrange("p (g d) -> p g d", g=NKV),
                                          bias[:, C_KV:C_KV + KV].rearrange("p (g d) -> p g d", g=NKV),
                                          ALU.add).then_inc(k_split, 1)
                        dve.tensor_tensor(v_all[:, bass.ds(t, 1), :], p_kv[:, KV:2 * KV].unsqueeze(1),
                                          bias[:, C_KV + KV:C_GATE].unsqueeze(1), ALU.add)
                        dve.tensor_copy(logits[:, bass.ds(t, 1), :], p_kv[:, 2 * KV:2 * KV + E].unsqueeze(1))
                        dve.wait_ge(k_split, 4 * t + 1)
                        dve.tensor_copy(k_aug[:, :, 0:DH], k_raw[:]).then_inc(k_split, 1)
                        dve.tensor_copy(k_aug[:, :, DH:2 * DH], k_raw[:]).then_inc(k_split, 1)
                        dve.wait_ge(k_split, 4 * t + 3)
                        dve.tensor_tensor(k_aug[:, :, 2 * DH:3 * DH], k_raw[:], k_aug[:, :, 0:DH],
                                          ALU.subtract).then_inc(k_split, 1)
                        wait(dve, q_stored, 16 * t)
                        dve.tensor_tensor(q_sb[:], p_q[:], bias[:, 0:D], ALU.add).then_inc(qkv_out, 1)
                    if after:
                        normalise(t + 1)
                        xT_lo(t + 1)
                    if here:
                        dve.wait_ge(silu_done, t + 1)
                        wait(dve, hT_done, t)
                        dve.tensor_tensor(h[:, 0:HS].rearrange("p (a n) -> p a n", a=2), p_u,
                                          act_g[:].rearrange("p (a n) -> p a n", a=2), ALU.mult).then_inc(h_done, 1)
                    if before:
                        dve.wait_ge(dn_done, t)
                        dve.wait_ge(xr_ready, t)
                        if not (isinstance(t, int) and t < 2):
                            dve.wait_ge(y_stored, 16 * (t - 1))
                        dve.tensor_tensor(y_sb[:], p_dn[:], xr[:], ALU.add).then_inc(y_done, 1)

                steps(dve, body)

            @block.tensor
            def _(pe):
                def product(dst, lhs, rhs, chunks, k_rows=None):
                    n, last = 0, 3 * chunks - 1
                    for c in range(chunks):
                        rows = P if k_rows is None or c < chunks - 1 else k_rows
                        for a, b in ((0, 0), (0, 1), (1, 0)):
                            ins = pe.matmul(dst, lhs[a][0:rows, c, :], rhs[b](c, rows), start=(n == 0),
                                            stop=(n == last))
                            n += 1
                    return ins

                def transpose_x(t):
                    pe.wait_ge(xn_done, t + 1)
                    wait(pe, xTl_done, t)
                    for c in range(DK):
                        ins = pe.transpose(p_x[:, c, :], xn[:, c * P:(c + 1) * P], ident[:])
                    ins.then_inc(xT_done, 1)

                def columns(hi, lo, a, b):
                    return [lambda c, r, w=w: w[0:r, c, a:b] for w in (hi, lo)]

                pe.wait_ge(consts, 9)
                transpose_x(0)

                def body(t):
                    before, here, after = has(t)
                    if here:
                        if isinstance(t, int) and t == 0:
                            pe.wait_ge(w_lo, 1)
                        pe.wait_ge(xTl_done, t + 1)
                        wait(pe, qkv_out, t)
                        wait(pe, kT_out, t)
                        product(p_q[:], (xT_h, xT_l), columns(in_h, in_l, 0, D), DK)
                        product(p_kv[:, 0:C_END - C_KV], (xT_h, xT_l), columns(in_h, in_l, C_KV, C_END),
                                DK).then_inc(qkv_done, 1)
                    if before:
                        pe.wait_ge(h_done, t)
                        for c in range(SC):
                            ins = pe.transpose(p_hT[:, c, :], h[:, c * P:(c + 1) * P], ident[:])
                        ins.then_inc(hT_done, 1)
                    if here:
                        if isinstance(t, int) and t == 0:
                            pe.wait_ge(w_lo, 2)
                        for n in range(4):
                            if n == 2:
                                wait(pe, hTl_done, t)
                            ins = product(p_gu[:, n, 0:HS // 2], (xT_h, xT_l),
                                          columns(gu_h, gu_l, n * HS // 2, (n + 1) * HS // 2), DK)
                        ins.then_inc(gu_done, 1)
                        pe.wait_ge(k_split, 4 * (t + 1))
                        for g in range(NKV):
                            ins = pe.transpose(p_kT[:, g, :], k_aug[:, g, :].bitcast(F32), ident[:])
                        ins.then_inc(kT_done, 1)
                    if after:
                        transpose_x(t + 1)
                    if before:
                        if isinstance(t, int) and t == 1:
                            pe.wait_ge(w_lo, 4)
                        pe.wait_ge(hTl_done, t)
                        if not (isinstance(t, int) and t < 2):
                            pe.wait_ge(y_done, t - 1)
                        product(p_dn[:], (hT_h, hT_l), columns(dn_h, dn_l, 0, D), SC, S_REST).then_inc(dn_done, 1)

                steps(pe, body)

        with ExitStack() as ctx:
            def sb(name, shape, dt=F32):
                return ctx.enter_context(nc.sbuf_tensor(name, shape, dt))

            def sem(name):
                return ctx.enter_context(nc.semaphore(name))

            UNITS = B * GROUPS
            k_next = sb("k_next", [QROWS, T], F32R)
            k_cur = sb("k_cur", [QROWS, T], F32R)
            v_cur = sb("v_cur", [P, KT, DH])
            ones = sb("ones_v", [P, DH])
            q_raw = sb("q_raw", [P, 2, 4, P])
            q_aug = sb("q_aug", [P, 2, 4, HG, KROWS], F32R)
            q_stack = sb("q_stack", [QROWS, 2, NQB, HG, QB], F32R)
            chunk_max = sb("chunk_max", [P, 2, 4 * HG * NQB])
            row_max = sb("row_max", [P, 2, 4 * HG])
            max_aug = sb("max_aug", [P, 2, 2, 4 * HG], F32R)
            max_T = sb("max_T", [2 * 4 * HG, 2, P], F32R)
            RING = 4
            probs = sb("probs", [P, RING, HG, QB])
            prob_sum = sb("prob_sum", [P, 2, HG, QB])
            o_raw = sb("o_raw", [P, 2, QB])
            sum_raw = sb("sum_raw", [P, 2, QB])
            inv_sum = sb("inv_sum", [P, 2, QB])
            o_sb = sb("o_sb", [P, 2, QB])
            p_prep = ctx.enter_context(nc.psum_tensor("p_prep", [P, 2, 512], F32))
            p_sc = ctx.enter_context(nc.psum_tensor("p_sc", [P, HG, QB], F32))
            p_o = ctx.enter_context(nc.psum_tensor("p_o", [P, QB], F32))
            p_sum = ctx.enter_context(nc.psum_tensor("p_sum", [P, QB], F32))

            rank = sb("rank", [P, E])
            earlier = sb("earlier", [P, P])
            all_ones = sb("all_ones", [P, P])
            zeros = sb("zeros", [P, TILES])
            tile_start = sb("tile_start", [P, SLOT_TILES])
            score = sb("score", [P, TILES, E])
            tmp = sb("tmp", [P, TILES, E])
            left = sb("left", [P, TILES, E])
            chosen = sb("chosen", [P, 2, TILES, E])
            both = sb("both", [P, TILES, E])
            col = sb("col", [P, 3, TILES])
            upto = sb("upto", [P, TILES, E])
            within = sb("within", [P, TILES, E])
            whole = sb("whole", [P, TILES, E])
            cnt = sb("cnt", [P, 4, E])
            cnt_i = sb("cnt_i", [P, 2, E], I32)
            owner = sb("owner", [P, E, SLOT_TILES])
            slot_f = sb("slot_f", [P, 2, TILES])
            zero_slots = sb("zero_slots", [P, SLOT_TILES], I32)
            p_within = p_o[:, 0:TILES * E].rearrange("p (t e) -> p t e", e=E)
            p_whole = p_sum[:, 0:TILES * E].rearrange("p (t e) -> p t e", e=E)
            made, step, score_exp, counted = sem("made"), sem("step"), sem("score_exp"), sem("counted")
            score_ready, both_ready = sem("score_ready"), sem("both_ready")
            cleared = sem("cleared")


            def over_e(ap):
                return ap.unsqueeze(2).to_broadcast([P, TILES, E])

            rows_set, k_loaded = sem("rows_set"), sem("k_loaded")
            k_copied, v_copied = sem("k_copied"), sem("v_copied")
            q_loaded = [sem("q_loaded0"), sem("q_loaded1")]
            split_step, q_split = sem("split_step"), sem("q_split")
            prep_made, s_read, t_read = sem("prep_made"), sem("s_read"), sem("t_read")
            fin_step, max_done, aug_read = sem("fin_step"), sem("max_done"), sem("aug_read")
            max_set = sem("max_set")
            sc_done, exp_done, pv_done, added = sem("sc_done"), sem("exp_done2"), sem("pv_done"), sem("added")
            o_out, inv_done, o_ready = sem("o_out"), sem("inv_done"), sem("o_ready")
            slots_loaded = sem("slots_loaded")
            scattered, passed, routed = sem("scattered"), sem("passed_a"), sem("routed")
            o_stored = [sem("o_stored0"), sem("o_stored1")]

            def preparation():
                by_block = [[("s", qb, h_, qt, c) for h_ in range(HG) for qt in range(4) for c in range(qb + 1)]
                            for qb in range(NQB)]
                first = [[("t1", qb, h_) for h_ in range(HG)] for qb in range(NQB)]
                last = [[("m", qb)] for qb in range(NQB)]

                def between(pieces, among):
                    out_ = list(among[:4])
                    for j in range(max(len(pieces), len(among) - 4)):
                        out_ += pieces[j:j + 1] + among[4 + j:5 + j]
                    return out_

                order = first[0][:2]
                for qb in range(NQB):
                    work, behind = by_block[qb], last[qb - 1] if qb else []
                    if qb == 0:
                        work = work[:4] + first[0][2:3] + work[4:8] + first[0][3:4] + work[8:]
                    work = between(behind, work)
                    ends = len(work) - 2 * HG
                    later = first[qb + 1] if qb + 1 < NQB else []
                    order = order + work[:ends] + between(later, work[ends:]) + [("fin", qb)]
                return order + last[NQB - 1]

            PREP = preparation()
            NUMBER = {}
            for a in PREP:
                if a[0] != "fin":
                    NUMBER[a] = len(NUMBER)
            ATOMS = len(NUMBER)
            ORDER = sorted(NUMBER, key=NUMBER.get)
            TURN, N_S, N_T = {}, 0, 0
            for a in ORDER:
                if a[0] == "s":
                    TURN[a], N_S = N_S, N_S + 1
                else:
                    TURN[a], N_T = N_T, N_T + 1
            STEPS = [(qb, kt) for qb in range(NQB) for kt in range(4 * (qb + 1))]
            NS = len(STEPS)
            assert ATOMS % 2 == 0 and NS % 2 == 0

            def q_first(qb, kt):
                return max(kt - 4 * qb, 0) * P

            BY_POOL = [s for s, (qb, kt) in enumerate(STEPS) if kt < 4 * qb and kt % 3 != 2]
            ADDS = [s for s in BY_POOL if STEPS[s][1] > 0]
            N_ADD = len(ADDS)
            assert NS % RING == 0 and not any(s in BY_POOL for s in range(NS - RING, NS))

            def probs_of(s):
                qb, kt = STEPS[s]
                return prob_sum[:, qb % 2] if s in BY_POOL and kt == 0 else probs[:, s % RING]

            def adds_upto(s):
                return len([a for a in ADDS if a < s])

            def spread(work, over):
                cost = [(QB - q_first(*STEPS[s])) * (2 if s in BY_POOL else 3) for s in over]
                total, given, so_far, out_ = sum(cost), 0, 0, {}
                for s, c in zip(over, cost):
                    so_far += c
                    upto_ = -(-len(work) * so_far // total)
                    out_[s] = work[given:upto_]
                    given = upto_
                return out_

            next_unit = [(1, a) for a in PREP[:-1]]
            left_over = [(0, PREP[-1])]
            BEHIND = 6
            made_by = [0] + [PREP.index(("m", qb)) + 1 + BEHIND for qb in range(NQB)]
            ahead = PREP[:made_by[1]]

            beside = spread(left_over + next_unit, range(NS))
            starts = [STEPS.index((qb, 0)) for qb in range(NQB)] + [NS]
            beside_first = {}
            for qb in range(NQB):
                span = range(starts[qb], starts[qb + 1])
                own = [(0, a) for a in PREP[made_by[qb + 1]:made_by[qb + 2]]] if qb + 1 < NQB else next_unit
                beside_first.update(spread(own, span))
            beside_last = {s: left_over[s:s + 1] for s in range(NS)}

            def layout(s, mine):
                more = s + 1 < NS
                parts = [[("scores", 0), ("scores", 1)], [("scores", 2), ("scores", 3)]] if more else []
                parts += [[("weigh", 0)]] if s in BY_POOL else [[("weigh", 0)], [], [("weigh", 1)]]
                own = any(ahead_by == 0 for ahead_by, _ in mine)
                gaps = 1 if own and more and STEPS[s + 1][1] == 0 else len(parts)
                out_ = []
                for j, part in enumerate(parts):
                    if j < gaps:
                        out_ += [("piece", x) for x in mine[-(-len(mine) * j // gaps):-(-len(mine) * (j + 1) // gaps)]]
                    out_ += part
                return out_

            def units(eng, pair):
                pair(0, (beside_first, beside))
                with eng.Fori(1, UNITS // 2 - 1) as i:
                    pair(i, (beside, beside))
                pair(UNITS // 2 - 1, (beside, beside_last))

            def keys_of(half, ahead_by):
                return k_next if half == 1 and ahead_by == 1 else k_cur

            block = ctx.enter_context(nc.Block())

            @block.sync
            def _(sp):
                sp.wait_ge(rows_set, 2)
                sp.dma_start(k_next[0:KROWS, :].bitcast(F32), k_d[:, 0, :]).then_inc(k_loaded, 16)

                def load_q(u, qb):
                    slot = qb % 2
                    wait(sp, q_split, 4 * u + qb - 1)
                    src = q_d.rearrange("t p d -> p t d")[:, bass.ds(u // GROUPS * KT + 4 * qb, 4),
                                                          bass.ds(u % GROUPS * P, P)]
                    sp.dma_start(q_raw[:, slot], src).then_inc(q_loaded[slot], 16)

                def store_o(u, qb):
                    sp.wait_ge(o_ready, 4 * u + qb + 1)
                    dst = at_d[bass.ds(u, 1), :, qb * QB:(qb + 1) * QB].rearrange("a p q -> (a p) q")
                    sp.dma_start(dst, o_sb[:, qb % 2]).then_inc(o_stored[qb % 2], 16)

                for qb in range(NQB):
                    load_q(0, qb)
                for qb in range(NQB):
                    load_q(1, qb)

                def pair(i, work):
                    for half in range(2):
                        u = 2 * i + half
                        if half == 0 and not (isinstance(i, int) and i == UNITS // 2 - 1):
                            sp.wait_ge(k_copied, NQB * (i + 1))
                            sp.wait_ge(v_copied, i + 1)
                            if isinstance(i, int):
                                sp.wait_ge(s_read, len([a for a in ahead if a[0] == "s"]))
                            sp.dma_start(k_next[0:KROWS, :].bitcast(F32), k_d[:, bass.ds(i + 1, 1), :].rearrange(
                                "r a t -> r (a t)")).then_inc(k_loaded, 16)
                        more = work[1] is not beside_last
                        for qb in range(NQB):
                            if more and qb > 0:
                                load_q(u + 2, qb - 1)
                            if more and qb == NQB - 1:
                                load_q(u + 2, qb)
                            store_o(u, qb)

                units(sp, pair)
                for s in o_stored:
                    sp.wait_ge(s, 16 * 2 * UNITS)

            @block.gpsimd
            def _(pool):
                pool.iota(rank[:], [[-1, E]], base=E, channel_multiplier=0,
                          allow_small_or_imprecise_dtypes=True).then_inc(made, 1)
                pool.iota(tile_start[:], [[P, SLOT_TILES]], base=0, channel_multiplier=0,
                          allow_small_or_imprecise_dtypes=True).then_inc(made, 1)
                pool.iota(token[:], [[P, TILES]], base=0, channel_multiplier=1).then_inc(made, 1)
                pool.memset(all_ones[:], 1.0).then_inc(made, 1)
                pool.memset(zeros[:], 0.0).then_inc(made, 1)
                pool.memset(zero_slots[:], 0).then_inc(made, 1)
                pool.wait_ge(made, 6)
                pool.affine_select(out=earlier[:], in_=all_ones[:], pattern=[[1, P]], compare_op=ALU.is_gt, fill=0.0,
                                   base=0, channel_multiplier=-1).then_inc(made, 1)
                pool.dma_start(slot_d.rearrange("(p t) o -> p (t o)", p=P), zero_slots[:]).then_inc(cleared, 16)

                def split(u, qb):
                    slot = qb % 2
                    pool.wait_ge(q_loaded[slot], 16 * (2 * u + qb // 2 + 1))
                    wait(pool, aug_read, 4 * u + qb - 1)
                    pool.sem_inc(passed, 1)
                    raw = q_raw[:, slot].rearrange("p t (h d) -> p t h d", h=HG)
                    pool.tensor_copy(q_aug[:, slot, :, :, 0:DH], raw).then_inc(split_step, 1)
                    pool.tensor_copy(q_aug[:, slot, :, :, 2 * DH:3 * DH], raw).then_inc(split_step, 1)
                    pool.wait_ge(split_step, 2 * (4 * u + qb + 1))
                    pool.tensor_tensor(q_aug[:, slot, :, :, DH:2 * DH], raw, q_aug[:, slot, :, :, 0:DH],
                                       ALU.subtract).then_inc(q_split, 1)

                def weigh_out(u, qb):
                    n, slot = 4 * u + qb, qb % 2
                    pool.wait_ge(inv_done, 4 * (n + 1))
                    wait(pool, o_stored[slot], 16 * (2 * u + qb // 2))
                    pool.tensor_tensor(o_sb[:, slot], o_raw[:, slot], inv_sum[:, slot], ALU.mult).then_inc(o_ready, 1)

                def splits(u, pieces):
                    for ahead_by, a in pieces:
                        if a[0] == "t1" and a[2] == HG - 1:
                            v, qb = u + ahead_by + (a[1] + 2) // NQB, (a[1] + 2) % NQB
                            if not (isinstance(v, int) and v >= UNITS):
                                split(v, qb)

                def add(u, s):
                    qb = STEPS[s][0]
                    pool.wait_ge(exp_done, 2 * (NS * u + s) + 2)
                    if s == min(a for a in ADDS if STEPS[a][0] == qb):
                        pool.wait_ge(pv_done, NS * u + starts[qb] + 1)
                    else:
                        pool.wait_ge(added, N_ADD * u + adds_upto(s))
                    pool.tensor_tensor(prob_sum[:, qb % 2], prob_sum[:, qb % 2], probs_of(s), ALU.add
                                       ).then_inc(added, 1)

                split(0, 0)
                split(0, 1)
                splits(0, [(0, a) for a in ahead])
                pool.wait_ge(cleared, 16)
                pool.wait_ge(routed, 1)
                scatters = [(c, t) for c in range(2) for t in range(TILES)]
                assert len(scatters) <= 2 * NS

                def pair(i, work):
                    first_pair = isinstance(i, int) and i == 0
                    for half in range(2):
                        u = 2 * i + half
                        for s, (qb, kt) in enumerate(STEPS):
                            if kt == 2 and qb > 0:
                                weigh_out(u, qb - 1)
                            elif kt == 2 and not (isinstance(u, int) and u == 0):
                                weigh_out(u - 1, NQB - 1)
                            if s in ADDS:
                                add(u, s)
                            splits(u, work[half][s])
                            for c, t in scatters[half * NS + s:half * NS + s + 1] if first_pair else []:
                                pool.indirect_dma_start(slot_d, bass.IndirectOffsetOnAxis(
                                    row_i[:, 1, c, t:t + 1], 0), token[:, t:t + 1], None).then_inc(scattered, 16)
                    if first_pair:
                        pool.wait_ge(scattered, 16 * len(scatters))

                units(pool, pair)
                pool.dma_start(slot_token[:], slot_d.rearrange("(p t) o -> p (t o)", p=P)).then_inc(slots_loaded, 16)
                pool.wait_ge(slots_loaded, 16)
                weigh_out(UNITS - 1, NQB - 1)

            @block.scalar
            def _(act):
                act.wait_ge(score_ready, 1)
                act.activation(score[:], tmp[:], ACT.Exp).then_inc(score_exp, 1)

                def take_out(u, qb):
                    slot = qb % 2
                    act.wait_ge(pv_done, NS * u + starts[qb + 1])
                    wait(act, o_ready, 4 * u + qb - 1)
                    act.activation(o_raw[:, slot], p_o[:], ACT.Copy).then_inc(o_out, 1)
                    act.activation(sum_raw[:, slot], p_sum[:], ACT.Copy).then_inc(o_out, 1)

                def weights(u, s, pr):
                    q0 = q_first(*STEPS[s])
                    act.wait_ge(sc_done, 2 * (NS * u + s) + pr + 1)
                    wait(act, pv_done, NS * u + s - RING + 1)
                    if s - RING in ADDS:
                        act.wait_ge(added, N_ADD * u + adds_upto(s - RING) + 1)
                    act.activation(probs_of(s)[:, 2 * pr:2 * pr + 2, q0:QB], p_sc[:, 2 * pr:2 * pr + 2, q0:QB],
                                   ACT.Exp, scale=SCALE).then_inc(exp_done, 1)

                def stack(u, parity, a):
                    n, qb = NUMBER[a], a[1]
                    act.wait_ge(prep_made, ATOMS * u + n + 1)
                    if a[0] == "t1":
                        act.activation(q_stack[0:KROWS, parity, qb, a[2], :], p_prep[0:KROWS, n % 2],
                                       ACT.Copy).then_inc(t_read, 1)
                        return
                    wait(act, max_set, 32 * (4 * u + qb))
                    act.activation(max_T[:, qb % 2], p_prep[0:2 * 4 * HG, n % 2, 0:P], ACT.Copy).then_inc(t_read, 1)
                    act.wait_ge(t_read, N_T * u + TURN[a] + 1)
                    for half_ in range(2):
                        row = q_stack[KROWS + half_:KROWS + half_ + 1, parity, qb]
                        act.dma_start(row.rearrange("a h (t q) -> a (h t) q", q=P).bitcast(F32),
                                      max_T[half_ * 4 * HG:(half_ + 1) * 4 * HG, qb % 2].bitcast(F32)
                                      ).then_inc(max_set, 16)

                for a in ahead:
                    if a[0] in ("t1", "m"):
                        stack(0, 0, a)

                def copy_keys(c):
                    act.activation(k_cur[0:KROWS, c * QB:(c + 1) * QB],
                                   k_next[0:KROWS, c * QB:(c + 1) * QB].bitcast(F32), ACT.Copy).then_inc(k_copied, 1)

                act.wait_ge(k_loaded, 16)
                for c in range(NQB):
                    copy_keys(c)

                def pair(i, work):
                    for half in range(2):
                        u = 2 * i + half
                        more = half == 1 and work[1] is not beside_last
                        for pr in range(2):
                            weights(u, 0, pr)
                        for s in range(NS):
                            for what, x in layout(s, work[half][s]):
                                if what == "scores" and x % 2 == 1:
                                    weights(u, s + 1, x // 2)
                                    qb, kt = STEPS[s + 1]
                                    if more and x == HG - 1 and qb == NQB - 1 and kt % 4 == 3:
                                        if kt == 3:
                                            act.wait_ge(k_loaded, 16 * (i + 2))
                                        copy_keys(kt // 4)
                                elif what == "piece" and x[1][0] in ("t1", "m"):
                                    stack(u + x[0], (half + x[0]) % 2, x[1])
                            if s + 1 in starts:
                                take_out(u, STEPS[s][0])

                units(act, pair)

            @block.vector
            def _(dve):
                FIN_STEPS = 2

                def atom(u, a):
                    qb = a[1]
                    if a[0] == "fin":
                        base = FIN_STEPS * (4 * u + qb)
                        dve.wait_ge(s_read, N_S * u + TURN[("s", qb, HG - 1, 3, qb)] + 1)
                        n = 4 * HG * (qb + 1)
                        dve.tensor_reduce(row_max[:, qb % 2], chunk_max[:, qb % 2, 0:n].rearrange(
                            "p (r c) -> p r c", c=qb + 1), AX.X, ALU.max).then_inc(fin_step, 1)
                        dve.wait_ge(fin_step, base + 1)
                        rows, hi, lo = row_max[:, qb % 2], max_aug[:, qb % 2, 0], max_aug[:, qb % 2, 1]
                        dve.tensor_scalar(hi, rows, -1.0, None, ALU.mult).then_inc(fin_step, 1)
                        dve.wait_ge(fin_step, base + 2)
                        dve.scalar_tensor_tensor(out=lo, in0=rows, scalar=-1.0, in1=hi, op0=ALU.mult,
                                                 op1=ALU.subtract).then_inc(max_done, 1)
                    elif a[0] == "s":
                        n = NUMBER[a]
                        dve.wait_ge(prep_made, ATOMS * u + n + 1)
                        _, qb, h_, qt, c = a
                        at = (h_ * 4 + qt) * (qb + 1) + c
                        keys = 512 if c < qb else (qt + 1) * P
                        dve.tensor_reduce(chunk_max[:, qb % 2, at:at + 1], p_prep[:, n % 2, 0:keys], AX.X,
                                          ALU.max).then_inc(s_read, 1)

                def beside_step(u, atoms):
                    for ahead_by, a in atoms:
                        atom(u + ahead_by, a)

                def invert(u, qb, piece):
                    n, slot, w = 4 * u + qb, qb % 2, QB // 4
                    if piece == 0:
                        dve.wait_ge(o_out, 2 * (n + 1))
                        wait(dve, o_ready, n - 1)
                    dve.reciprocal(inv_sum[:, slot, piece * w:(piece + 1) * w],
                                   sum_raw[:, slot, piece * w:(piece + 1) * w]).then_inc(inv_done, 1)

                dve.memset(k_next[KROWS:QROWS, :].bitcast(F32), 1.0).then_inc(rows_set, 1)
                dve.memset(k_cur[KROWS:QROWS, :].bitcast(F32), 1.0).then_inc(rows_set, 1)
                dve.memset(ones[:], 1.0).then_inc(rows_set, 1)
                n = 0

                def done(ins):
                    nonlocal n
                    n += 1
                    ins.then_inc(step, 1)
                    dve.wait_ge(step, n)

                done(dve.tensor_reduce(col[:, 0, :], logits[:], AX.X, ALU.max))
                dve.tensor_tensor(tmp[:], logits[:], over_e(col[:, 0, :]), ALU.subtract).then_inc(score_ready, 1)
                dve.wait_ge(score_exp, 1)
                done(dve.tensor_reduce(col[:, 1, :], score[:], AX.X, ALU.add))
                done(dve.reciprocal(col[:, 2, :], col[:, 1, :]))
                done(dve.tensor_tensor(left[:], score[:], over_e(col[:, 2, :]), ALU.mult))
                dve.wait_ge(made, 7)
                for c in range(2):
                    done(dve.tensor_reduce(weight_of[:, c, :], left[:], AX.X, ALU.max))
                    done(dve.tensor_tensor(tmp[:], left[:], over_e(weight_of[:, c, :]), ALU.is_equal))
                    done(dve.tensor_tensor(tmp[:], tmp[:], rank[:].unsqueeze(1).to_broadcast([P, TILES, E]),
                                           ALU.mult))
                    done(dve.tensor_reduce(col[:, 0, :], tmp[:], AX.X, ALU.max))
                    done(dve.tensor_tensor(chosen[:, c], tmp[:], over_e(col[:, 0, :]), ALU.is_equal))
                    if c == 0:
                        done(dve.scalar_tensor_tensor(out=left[:], in0=chosen[:, 0], scalar=-2.0, in1=left[:],
                                                      op0=ALU.mult, op1=ALU.add))
                dve.tensor_tensor(both[:], chosen[:, 0], chosen[:, 1], ALU.add).then_inc(both_ready, 1)
                dve.wait_ge(counted, 2)
                done(dve.tensor_copy(whole[:], p_whole))
                for e in range(E):
                    done(dve.tensor_tensor_scan(upto[:, :, e], whole[:, :, e], zeros[:], 0.0, ALU.add, ALU.add))
                done(dve.tensor_tensor(within[:], upto[:], whole[:], ALU.subtract))
                done(dve.tensor_tensor(within[:], within[:], p_within, ALU.add))
                done(dve.tensor_scalar_add(cnt_i[:, 0, :], upto[:, TILES - 1, :], float(P - 1)))
                done(dve.tensor_scalar(cnt_i[:, 1, :], cnt_i[:, 0, :], P.bit_length() - 1, None,
                                       ALU.logical_shift_right))
                done(dve.tensor_scalar(cnt[:, 0, :], cnt_i[:, 1, :], float(P), None, ALU.mult))
                done(dve.tensor_tensor_scan(cnt[:, 1, :], cnt[:, 0, :], zeros[:, 0:E], 0.0, ALU.add, ALU.add))
                done(dve.tensor_tensor(cnt[:, 2, :], cnt[:, 1, :], cnt[:, 0, :], ALU.subtract))
                done(dve.tensor_tensor(within[:], within[:],
                                       cnt[:, 2, :].unsqueeze(1).to_broadcast([P, TILES, E]), ALU.add))
                for c in range(2):
                    done(dve.tensor_tensor(tmp[:], chosen[:, c], within[:], ALU.mult))
                    done(dve.tensor_reduce(slot_f[:, c, :], tmp[:], AX.X, ALU.add))
                done(dve.tensor_copy(slot_of[:], slot_f[:]))
                done(dve.tensor_scalar(row_i[:, 0], slot_of[:], P.bit_length() - 1, None, ALU.logical_shift_right))
                done(dve.tensor_scalar(slot_f[:], slot_f[:], float(SLOT_TILES), None, ALU.mult))
                dve.scalar_tensor_tensor(out=row_i[:, 1], in0=row_i[:, 0], scalar=float(1 - P * SLOT_TILES),
                                         in1=slot_f[:], op0=ALU.mult, op1=ALU.add)
                done(dve.tensor_scalar(owner[:, 0, :], tile_start[:], cnt[:, 1, 0:1], None, ALU.is_ge))
                for e in range(1, E - 1):
                    done(dve.scalar_tensor_tensor(out=owner[:, e, :], in0=tile_start[:], scalar=cnt[:, 1, e:e + 1],
                                                  in1=owner[:, e - 1, :], op0=ALU.is_ge, op1=ALU.add))
                dve.tensor_copy(expert_of[:], owner[:, E - 2, :]).then_inc(routed, 1)

                for a in ahead:
                    atom(0, a)

                def pair(i, work):
                    wait(dve, pv_done, NS * 2 * i)
                    dve.tensor_copy(v_cur[:], v_all[:, bass.ds(2 * i // GROUPS * KT, KT),
                                                    bass.ds(i % NKV * DH, DH)]).then_inc(v_copied, 1)
                    for half in range(2):
                        u = 2 * i + half
                        for s, (qb, kt) in enumerate(STEPS):
                            atoms = work[half][s]
                            if s - 1 in starts and not (isinstance(u, int) and u == 0 and s == 1):
                                cut = [len(atoms) * j // 4 for j in range(5)]
                                for j in range(4):
                                    invert(*((u, qb - 1) if qb else (u - 1, NQB - 1)), j)
                                    beside_step(u, atoms[cut[j]:cut[j + 1]])
                            else:
                                beside_step(u, atoms)

                units(dve, pair)
                for j in range(4):
                    invert(UNITS - 1, NQB - 1, j)

            @block.tensor
            def _(pe):
                def atom(u, half, ahead_by, a):
                    if a[0] == "fin":
                        return
                    n, qb, slot, par = NUMBER[a], a[1], a[1] % 2, (half + ahead_by) % 2
                    u = u + ahead_by
                    before = ORDER[n - 2]
                    turns, read = (N_S, s_read) if before[0] == "s" else (N_T, t_read)
                    wait(pe, read, turns * (u if n >= 2 else u - 1) + TURN[before] + 1)
                    bank = p_prep[:, n % 2]
                    if a[0] == "s":
                        _, qb, h_, qt, c = a
                        pe.wait_ge(t_read, N_T * u + TURN[("t1", qb, h_)] + 1)
                        keys = keys_of(half, ahead_by) if keys_from is None else keys_from
                        lhs = q_stack[0:KROWS, par, qb, h_, qt * P:(qt + 1) * P]
                        if c < qb:
                            ins = pe.matmul(bank[:, 0:512], lhs, keys[0:KROWS, c * 512:(c + 1) * 512], start=True,
                                            stop=True)
                        else:
                            pe.matmul(bank[:, 0:(qt + 1) * P], lhs, keys[0:KROWS, c * 512:c * 512 + (qt + 1) * P],
                                      start=True, stop=False)
                            ins = pe.matmul(bank[:, qt * P:(qt + 1) * P], ident16[:], below16[:], start=False,
                                            stop=True)
                    elif a[0] == "t1":
                        _, qb, h_ = a
                        pe.wait_ge(q_split, 4 * u + qb + 1)
                        for qt in range(4):
                            ins = pe.transpose(bank[0:KROWS, qt * P:(qt + 1) * P],
                                               q_aug[:, slot, qt, h_, :].bitcast(F32), ident[:])
                        if h_ == HG - 1:
                            ins.then_inc(prep_made, 1)
                            pe.wait_ge(prep_made, ATOMS * u + n + 1)
                            pe.sem_inc(aug_read, 1)
                            return
                    else:
                        pe.wait_ge(max_done, 4 * u + qb + 1)
                        ins = pe.transpose(bank[0:2 * 4 * HG, 0:P], max_aug[:, slot].rearrange(
                            "p a n -> p (a n)").bitcast(F32), ident[:])
                    ins.then_inc(prep_made, 1)

                def scores(u, half, s, h_):
                    qb, kt = STEPS[s]
                    q0 = q_first(qb, kt)
                    if kt == 0 and h_ == 0:
                        pe.wait_ge(max_set, 32 * (4 * u + qb + 1))
                    if h_ % 2 == 0:
                        wait(pe, exp_done, 2 * (NS * u + s) + h_ // 2 - 1)
                    diagonal = kt >= 4 * qb
                    ins = pe.matmul(p_sc[:, h_, q0:QB], k_cur[:, kt * P:(kt + 1) * P],
                                    q_stack[:, half, qb, h_, q0:QB], start=True,
                                    stop=not diagonal)
                    if diagonal:
                        ins = pe.matmul(p_sc[:, h_, q0:q0 + P], ident16[:], above16[:], start=False, stop=True)
                    if h_ % 2 == 1:
                        ins.then_inc(sc_done, 1)

                def weigh(u, s, dst, lhs):
                    qb, kt = STEPS[s]
                    q0 = q_first(qb, kt)
                    if dst is p_o:
                        pe.wait_ge(exp_done, 2 * (NS * u + s) + 2)
                    n = 4 * u + qb
                    first = s == min(a for a in range(starts[qb], NS) if dst is p_o or a not in BY_POOL)
                    last = s + 1 == starts[qb + 1]
                    if first and not (isinstance(n, int) and n == 0):
                        pe.wait_ge(o_out, 2 * n - (dst is p_o))
                    if dst is p_sum and last and qb > 0:
                        pe.wait_ge(added, N_ADD * u + adds_upto(s))
                        for h_ in range(HG):
                            pe.matmul(dst[h_ * DH:(h_ + 1) * DH, :], lhs, prob_sum[:, qb % 2, h_, :], start=False,
                                      stop=False)
                    for h_ in range(HG):
                        ins = pe.matmul(dst[h_ * DH:(h_ + 1) * DH, q0:QB], lhs, probs_of(s)[:, h_, q0:QB],
                                        start=first, stop=last)
                    if dst is p_sum or s in BY_POOL:
                        ins.then_inc(pv_done, 1)

                pe.wait_ge(made, 7)
                pe.wait_ge(both_ready, 1)
                pe.matmul(p_within, earlier[:], both[:], start=True, stop=True).then_inc(counted, 1)
                pe.matmul(p_whole, all_ones[:], both[:], start=True, stop=True).then_inc(counted, 1)

                keys_from = k_next
                pe.wait_ge(rows_set, 3)
                pe.wait_ge(k_loaded, 16)
                for a in ahead:
                    atom(0, 0, 0, a)
                keys_from = None

                def pair(i, work):
                    for half in range(2):
                        u = 2 * i + half
                        if half == 0:
                            pe.wait_ge(k_copied, NQB * i + 1)
                        for h_ in range(HG):
                            scores(u, half, 0, h_)
                        if half == 0:
                            pe.wait_ge(k_copied, NQB * (i + 1))
                        if half == 1 and work[1] is not beside_last:
                            pe.wait_ge(k_loaded, 16 * (i + 2))
                        for s in range(NS):
                            for what, x in layout(s, work[half][s]):
                                if what == "piece":
                                    atom(u, half, *x)
                                elif what == "scores":
                                    scores(u, half, s + 1, x)
                                elif x == 0:
                                    if half == 0 and s == 0:
                                        pe.wait_ge(v_copied, i + 1)
                                    weigh(u, s, p_o, v_cur[:, STEPS[s][1], :])
                                else:
                                    weigh(u, s, p_sum, ones[:])

                units(pe, pair)

        with ExitStack() as ctx:
            def sb(name, shape, dt=F32):
                return ctx.enter_context(nc.sbuf_tensor(name, shape, dt))

            def pb(name, shape):
                return ctx.enter_context(nc.psum_tensor(name, shape, F32))

            def sem(name):
                return ctx.enter_context(nc.semaphore(name))

            w_gu = sb("w_gu", [P, E, DK, 2, H])
            w_dn = sb("w_dn", [P, E, HC, D])
            gu_h, gu_l = sb("gu_hr", [P, DK, 2, H], F32R), sb("gu_lr", [P, DK, 2, H], F32R)
            dn_h, dn_l = sb("dn_hr", [P, HC, D], F32R), sb("dn_lr", [P, HC, D], F32R)
            index = sb("index", [P, 2], I32)
            xg = sb("xg", [P, 2, D])
            xT_h, xT_l = sb("xT_hr", [P, DK, P], F32R), sb("xT_lr", [P, DK, P], F32R)
            act_g = sb("act_gr", [P, H])
            h = sb("h_r", [P, HC * P])
            hT_h, hT_l = sb("hT_hr", [P, HC, P], F32R), sb("hT_lr", [P, HC, P], F32R)
            ye = sb("ye", [P, D])
            p_x = pb("p_xr", [P, DK, P])
            p_g, p_u = pb("p_gr", [P, 512]), pb("p_ur", [P, 512])
            p_hT = pb("p_hTr", [P, HC, P])
            p_y = pb("p_yr", [P, D])
            w_loaded = [sem("w_loaded_even"), sem("w_loaded_odd")]
            padded = sem("padded")
            passed = sem("passed_r")
            passed_act, passed_dve, passed_pool = sem("passed_act"), sem("passed_dve"), sem("passed_pool")
            index_set, gathered = sem("index_set"), [sem("gathered0"), sem("gathered1")]
            gu_hi, gu_lo, gu_used = sem("gu_hi"), sem("gu_lo"), sem("gu_used")
            dn_hi, dn_lo = sem("dn_hi"), sem("dn_lo")
            xT_done, xTh_done, xTl_done = sem("xT_done_r"), sem("xTh_done_r"), sem("xTl_done_r")
            silu_done, h_done = sem("silu_done_r"), sem("h_done_r")
            hT_done, hTh_done, hTl_done = sem("hT_done_r"), sem("hTh_done_r"), sem("hTl_done_r")
            y_done, y_out, y_stored = sem("y_done_r"), sem("y_out_r"), sem("y_stored_r")
            W_DMAS = 4
            EARLY, REST = range(0, 2), range(2, DK)

            def both_slots(eng, body):
                body(0, 0)
                body(1, 1)
                with eng.Fori(1, SLOT_TILES // 2 - 1) as i:
                    body(2 * i, 0)
                    body(2 * i + 1, 1)
                body(SLOT_TILES - 2, 0)
                body(SLOT_TILES - 1, 1)
                body(SLOT_TILES, 0)

            def has(t):
                if not isinstance(t, int):
                    return True, True, True
                return t >= 1, t < SLOT_TILES, t + 1 < SLOT_TILES

            def expert(eng, t, passed_):
                eng.sem_inc(passed_, 1)
                return eng.value_load(expert_of[0:1, bass.ds(t, 1)], min_val=0, max_val=E - 1)

            assert SLOT_TILES % 2 == 0
            block = ctx.enter_context(nc.Block())

            @block.sync
            def _(sp):
                for e in range(E):
                    landed = w_loaded[e % 2]
                    if e > 1:
                        sp.wait_ge(landed, 16 * W_DMAS * (e // 2) + e % 2)
                    sp.dma_start(w_gu[:, e, :, 0, :], w_gate[e].rearrange("(k p) n -> p k n", p=P)
                                 ).then_inc(landed, 16)
                    sp.dma_start(w_gu[:, e, :, 1, :], w_up[e].rearrange("(k p) n -> p k n", p=P)
                                 ).then_inc(landed, 16)
                    sp.dma_start(w_dn[:, e, 0:HC - 1, :], w_down[e, 0:(HC - 1) * P, :].rearrange(
                        "(k p) n -> p k n", p=P)).then_inc(landed, 16)
                    sp.dma_start(w_dn[0:H_REST, e, HC - 1, :], w_down[e, (HC - 1) * P:H, :]).then_inc(landed, 16)
                with sp.Fori(0, SLOT_TILES) as t:
                    sp.wait_ge(y_out, t + 1)
                    sp.dma_start(tile(ys_t, t), ye[:]).then_inc(y_stored, 16)
                sp.wait_ge(y_stored, 16 * SLOT_TILES)

            @block.gpsimd
            def _(pool):
                pool.memset(h[:, H:HC * P], 0.0).then_inc(padded, 1)
                def gather(t, k):
                    if not (isinstance(t, int) and t < 2):
                        pool.wait_ge(gathered[k], 16 * (t // 2))
                        wait_apart(pool, xT_done, t - 1, passed)
                    pool.tensor_copy(index[:, k:k + 1], slot_token[:, bass.ds(t, 1)]).then_inc(index_set, 1)
                    wait_apart(pool, index_set, t + 1, passed)
                    pool.indirect_dma_start(xg[:, k], None, xn_d, bass.IndirectOffsetOnAxis(index[:, k:k + 1], 0)
                                            ).then_inc(gathered[k], 16)

                gather(0, 0)
                gather(1, 1)

                def body(t, k):
                    if isinstance(t, int) and t == SLOT_TILES:
                        return
                    if not (isinstance(t, int) and t + 2 >= SLOT_TILES):
                        gather(t + 2, k)
                    e = expert(pool, t, passed_pool)
                    for c in range(HC):
                        r = P if c < HC - 1 else H_REST
                        pool.wait_ge(dn_hi, HC * t + c + 1)
                        pool.tensor_tensor(dn_l[0:r, c, :],
                                           w_dn[0:r, bass.ds(e, 1), c, :].rearrange("p a n -> p (a n)"),
                                           dn_h[0:r, c, :], ALU.subtract).then_inc(dn_lo, 1)

                both_slots(pool, body)

            @block.scalar
            def _(act):
                act.sem_inc(w_loaded[1], 1)

                def xT_hi(t):
                    act.wait_ge(xT_done, t + 1)
                    wait(act, gu_used, DK * t)
                    act.activation(xT_h[:], p_x[:], ACT.Copy).then_inc(xTh_done, 1)

                def landed(t):
                    e = expert(act, t, passed_act)
                    act.wait_ge(w_loaded[0], 16 * W_DMAS * (e // 2 + 1))
                    act.wait_ge(w_loaded[1], 16 * W_DMAS * ((e + 1) // 2) + 1)
                    return e

                def weights_gu(t, e, chunks):
                    for c in chunks:
                        wait(act, gu_used, DK * (t - 1) + c + 1)
                        act.activation(gu_h[:, c], w_gu[:, bass.ds(e, 1), c].rearrange("p a b n -> p (a b) n"),
                                       ACT.Copy).then_inc(gu_hi, 1)

                def weights_dn(t):
                    e = expert(act, t, passed_act)
                    wait(act, y_done, t)
                    for c in range(HC):
                        r = P if c < HC - 1 else H_REST
                        act.activation(dn_h[0:r, c, :], w_dn[0:r, bass.ds(e, 1), c, :].rearrange(
                            "p a n -> p (a n)"), ACT.Copy).then_inc(dn_hi, 1)

                xT_hi(0)
                weights_gu(0, landed(0), range(DK))

                def body(t, k):
                    before, here, after = has(t)
                    if before:
                        act.wait_ge(hT_done, t)
                        act.activation(hT_h[:], p_hT[:], ACT.Copy).then_inc(hTh_done, 1)
                    if after:
                        e = landed(t + 1)
                        weights_gu(t + 1, e, EARLY)
                    if here:
                        act.wait_ge(gu_used, DK * (t + 1))
                        wait(act, h_done, t)
                        act.activation(act_g[:], p_g[:, 0:H], ACT.Silu).then_inc(silu_done, 1)
                    if after:
                        xT_hi(t + 1)
                        weights_gu(t + 1, e, REST)
                    if here:
                        weights_dn(t)
                    if before:
                        act.wait_ge(y_done, t)
                        if not (isinstance(t, int) and t < 2):
                            act.wait_ge(y_stored, 16 * (t - 1))
                        act.activation(ye[:], p_y[:], ACT.Copy).then_inc(y_out, 1)

                both_slots(act, body)

            @block.vector
            def _(dve):
                dve.wait_ge(padded, 1)

                def xT_lo(t):
                    dve.wait_ge(xTh_done, t + 1)
                    dve.tensor_tensor(xT_l[:], p_x[:], xT_h[:], ALU.subtract).then_inc(xTl_done, 1)

                def weights_gu(t, e, chunks):
                    for c in chunks:
                        dve.wait_ge(gu_hi, DK * t + c + 1)
                        dve.tensor_tensor(gu_l[:, c], w_gu[:, bass.ds(e, 1), c].rearrange("p a b n -> p (a b) n"),
                                          gu_h[:, c], ALU.subtract).then_inc(gu_lo, 1)

                xT_lo(0)
                weights_gu(0, expert(dve, 0, passed_dve), range(DK))

                def body(t, k):
                    before, here, after = has(t)
                    if before:
                        dve.wait_ge(hTh_done, t)
                        dve.tensor_tensor(hT_l[:], p_hT[:], hT_h[:], ALU.subtract).then_inc(hTl_done, 1)
                    if after:
                        e = expert(dve, t + 1, passed_dve)
                        weights_gu(t + 1, e, EARLY)
                    if here:
                        dve.wait_ge(silu_done, t + 1)
                        wait(dve, hT_done, t)
                        dve.tensor_tensor(h[:, 0:H], p_u[:, 0:H], act_g[:], ALU.mult).then_inc(h_done, 1)
                    if after:
                        xT_lo(t + 1)
                        weights_gu(t + 1, e, REST)

                both_slots(dve, body)

            @block.tensor
            def _(pe):
                def transpose_x(t, k):
                    pe.wait_ge(gathered[k], 16 * (t // 2 + 1))
                    wait(pe, xTl_done, t)
                    for c in range(DK):
                        ins = pe.transpose(p_x[:, c, :], xg[:, k, c * P:(c + 1) * P], ident[:])
                    ins.then_inc(xT_done, 1)

                transpose_x(0, 0)

                def body(t, k):
                    before, here, after = has(t)
                    if before:
                        pe.wait_ge(h_done, t)
                        for c in range(HC):
                            ins = pe.transpose(p_hT[:, c, :], h[:, c * P:(c + 1) * P], ident[:])
                        ins.then_inc(hT_done, 1)
                    if here:
                        pe.wait_ge(xTl_done, t + 1)
                        for c in range(DK):
                            pe.wait_ge(gu_lo, DK * t + c + 1)
                            for n, dst in enumerate((p_g, p_u)):
                                for j, (xh, wh) in enumerate(((xT_h, gu_h), (xT_h, gu_l), (xT_l, gu_h))):
                                    ins = pe.matmul(dst[:, 0:H], xh[:, c, :], wh[:, c, n, :],
                                                    start=(c == 0 and j == 0), stop=(c == DK - 1 and j == 2))
                            ins.then_inc(gu_used, 1)
                    if after:
                        transpose_x(t + 1, 1 - k)
                    if before:
                        pe.wait_ge(hTl_done, t)
                        if not (isinstance(t, int) and t < 2):
                            pe.wait_ge(y_out, t - 1)
                        for c in range(HC):
                            r = P if c < HC - 1 else H_REST
                            pe.wait_ge(dn_lo, HC * (t - 1) + c + 1)
                            for j, (hh, wh) in enumerate(((hT_h, dn_h), (hT_h, dn_l), (hT_l, dn_h))):
                                ins = pe.matmul(p_y[:], hh[0:r, c, :], wh[0:r, c, :], start=(c == 0 and j == 0),
                                                stop=(c == HC - 1 and j == 2))
                        ins.then_inc(y_done, 1)

                both_slots(pe, body)

        with ExitStack() as ctx:
            def sb(name, shape, dt=F32):
                return ctx.enter_context(nc.sbuf_tensor(name, shape, dt))

            def sem(name):
                return ctx.enter_context(nc.semaphore(name))

            RING = 4
            wo = sb("wo", [P, GROUPS, D])
            wo_h, wo_l = sb("wo_h", [P, GROUPS, D], F32R), sb("wo_l", [P, GROUPS, D], F32R)
            at = sb("at", [P, RING, GROUPS, P])
            at_h, at_l = sb("at_h", [P, 2, GROUPS, P], F32R), sb("at_l", [P, 2, GROUPS, P], F32R)
            y_in = sb("y_in", [P, RING, D])
            index = sb("index_c", [P, RING, 2], I32)
            got = sb("got", [P, RING, 2, D])
            acc = sb("acc", [P, 2, 3, D])
            p_a = ctx.enter_context(nc.psum_tensor("p_a", [P, 2, D], F32))
            wo_loaded, wo_hi, wo_lo = sem("wo_loaded"), sem("wo_hi"), sem("wo_lo")
            at_loaded = [sem(f"at_loaded{k}") for k in range(RING)]
            y_loaded = [sem(f"y_loaded{k}") for k in range(RING)]
            got_loaded = [[sem(f"got_loaded{k}_{c}") for c in range(2)] for k in range(RING)]
            passed, index_set = sem("passed_c"), sem("index_set_c")
            at_hi, at_lo = sem("at_hi"), sem("at_lo")
            a_done, acc_step, out_done = sem("a_done"), sem("acc_step"), sem("out_done")
            out_stored = [sem("out_stored0"), sem("out_stored1")]

            def rounds(eng, body):
                for k in range(RING):
                    body(k, k)
                with eng.Fori(1, TILES // RING - 1) as i:
                    for k in range(RING):
                        body(RING * i + k, k)
                for k in range(RING):
                    body(TILES - RING + k, k)

            def beyond(t, n):
                return not (isinstance(t, int) and t < n)

            block = ctx.enter_context(nc.Block())

            @block.sync
            def _(sp):
                sp.dma_start(wo[:], Wo.rearrange("(k p) n -> p k n", p=P)).then_inc(wo_loaded, 16)

                def body(t, k):
                    if beyond(t, RING):
                        sp.wait_ge(at_lo, t - RING + 1)
                    src = at_d[bass.ds(t // KT * GROUPS, GROUPS), :, bass.ds(t % KT * P, P)].rearrange(
                        "g p q -> p g q")
                    sp.dma_start(at[:, k], src).then_inc(at_loaded[k], 16)
                    if beyond(t, RING):
                        sp.wait_ge(acc_step, 2 * (t - RING) + 1)
                    sp.dma_start(y_in[:, k], tile(y_d, t)).then_inc(y_loaded[k], 16)

                rounds(sp, body)

            @block.gpsimd
            def _(pool):
                def body(t, k):
                    if beyond(t, RING):
                        wait_apart(pool, out_done, t - RING + 1, passed)
                    pool.tensor_copy(index[:, k, :], slot_of[:, :, bass.ds(t, 1)].rearrange("p c a -> p (c a)")
                                     ).then_inc(index_set, 1)
                    wait_apart(pool, index_set, t + 1, passed)
                    for c in range(2):
                        pool.indirect_dma_start(got[:, k, c, :], None, ys_d,
                                                bass.IndirectOffsetOnAxis(index[:, k, c:c + 1], 0)
                                                ).then_inc(got_loaded[k][c], 16)

                rounds(pool, body)

            @block.tensor
            def _(pe):
                pe.wait_ge(wo_lo, 1)

                def body(t, k):
                    pe.wait_ge(at_lo, t + 1)
                    if beyond(t, 2):
                        pe.wait_ge(acc_step, 2 * (t - 2) + 1)
                    for g in range(GROUPS):
                        for j, (a_, w_) in enumerate(((at_h, wo_h), (at_h, wo_l), (at_l, wo_h))):
                            ins = pe.matmul(p_a[:, k % 2], a_[:, k % 2, g, :], w_[:, g, :],
                                            start=(g == 0 and j == 0), stop=(g == GROUPS - 1 and j == 2))
                    ins.then_inc(a_done, 1)

                rounds(pe, body)

            @block.vector
            def _(dve):
                dve.wait_ge(wo_hi, 1)
                dve.tensor_tensor(wo_l[:], wo[:], wo_h[:], ALU.subtract).then_inc(wo_lo, 1)

                def lower(t, k):
                    dve.wait_ge(at_hi, t + 1)
                    dve.tensor_tensor(at_l[:, k % 2], at[:, k], at_h[:, k % 2], ALU.subtract).then_inc(at_lo, 1)

                lower(0, 0)

                def body(t, k):
                    if not (isinstance(t, int) and t + 1 == TILES):
                        lower(t + 1, (k + 1) % RING)
                    s_ = k % 2
                    dve.wait_ge(a_done, t + 1)
                    dve.wait_ge(y_loaded[k], 16 * (t // RING + 1))
                    dve.tensor_tensor(acc[:, s_, 0, :], p_a[:, s_], y_in[:, k], ALU.add).then_inc(acc_step, 1)
                    dve.wait_ge(got_loaded[k][0], 16 * (t // RING + 1))
                    dve.wait_ge(acc_step, 2 * t + 1)
                    w = [weight_of[:, c, bass.ds(t, 1)] for c in range(2)]
                    dve.scalar_tensor_tensor(out=acc[:, s_, 1, :], in0=got[:, k, 0, :], scalar=w[0],
                                             in1=acc[:, s_, 0, :], op0=ALU.mult, op1=ALU.add).then_inc(acc_step, 1)
                    dve.wait_ge(got_loaded[k][1], 16 * (t // RING + 1))
                    dve.wait_ge(acc_step, 2 * t + 2)
                    if beyond(t, 2):
                        dve.wait_ge(out_stored[s_], 16 * (t // 2))
                    dve.scalar_tensor_tensor(out=acc[:, s_, 2, :], in0=got[:, k, 1, :], scalar=w[1],
                                             in1=acc[:, s_, 1, :], op0=ALU.mult, op1=ALU.add).then_inc(out_done, 1)

                rounds(dve, body)

            @block.scalar
            def _(act):
                act.wait_ge(wo_loaded, 16)
                act.activation(wo_h[:], wo[:], ACT.Copy).then_inc(wo_hi, 1)

                def upper(t, k):
                    act.wait_ge(at_loaded[k], 16 * (t // RING + 1))
                    if beyond(t, 2):
                        act.wait_ge(a_done, t - 1)
                    act.activation(at_h[:, k % 2], at[:, k], ACT.Copy).then_inc(at_hi, 1)

                def store(t, k):
                    act.wait_ge(out_done, t + 1)
                    act.dma_start(tile(ot, t), acc[:, k % 2, 2, :]).then_inc(out_stored[k % 2], 16)

                def body(t, k):
                    upper(t, k)
                    if beyond(t, 2):
                        store(t - 2, k)

                rounds(act, body)
                for t in (TILES - 2, TILES - 1):
                    store(t, t % RING)
                for s in out_stored:
                    act.wait_ge(s, 16 * TILES // 2)


_INS = ["L0_attn_x", "L0_attn_Wq", "L0_attn_bq", "L0_attn_Wk", "L0_attn_bk", "L0_attn_Wv", "L0_attn_bv",
        "L0_attn_Wo", "L0_attn_bo", "L0_ffn_gate_w", "L0_ffn_w_gate", "L0_ffn_w_up", "L0_ffn_w_down",
        "L0_ffn_sw_gate", "L0_ffn_sw_up", "L0_ffn_sw_down"]


def kernel(**inputs):
    import numpy as _np
    import concourse.bacc as _bacc
    from concourse import mybir as _mybir
    from concourse.bass_utils import run_bass_kernel_spmd as _run

    nc = _bacc.Bacc("TRN2", target_bir_lowering=False, num_devices=1)
    arrays, args = {}, []
    for name in _INS:
        a = _np.ascontiguousarray(inputs[name])
        arrays[f"in_{name}"] = a
        args.append(nc.dram_tensor(f"in_{name}", a.shape, _mybir.dt.from_np(a.dtype), kind="ExternalInput").ap())
    args.append(nc.dram_tensor("out_0", inputs["L0_attn_x"].shape, _mybir.dt.float32, kind="ExternalOutput").ap())
    layer_kernel(nc, *args)
    r = _run(nc, [arrays], core_ids=[0])
    return r.results[0]["out_0"]
```
